# Optimizing a Trainium2 kernel written in Bass

```python
import numpy as np
import jax
import jax.numpy as jnp

def _softmax(x, axis=-1):
    return jax.nn.softmax(x, axis=axis)

def _gelu(x):
    return jax.nn.gelu(x, approximate=True)

def _silu(x):
    return jax.nn.silu(x)

def _sigmoid(x):
    return jax.nn.sigmoid(x)

def _layernorm(x, axis=-1, eps=1e-05):
    m = jnp.mean(x, axis=axis, keepdims=True)
    v = jnp.var(x, axis=axis, keepdims=True)
    return (x - m) / jnp.sqrt(v + eps)

def _scatter_add(tgt, idx, src, axis=0):
    return tgt.at[idx].add(src)

def _segment_sum(src, seg, n):
    return jax.ops.segment_sum(src, seg, n)
kernel_name = 'mk_seq_preln_d2_jaxref_r8_95cc84'

def setup_inputs(seed: int=0):
    np.random.seed(seed)
    _w = jnp.asarray

    def _L0_attn_setup():
        import jax, jax.numpy as jnp
        import numpy as np
        N, L, E, H = (4, 512, 128, 128)
        key = jax.random.key(seed)
        ks = jax.random.split(key, 7)
        s_in = 1.0 / np.sqrt(E)
        return {'X_embed': jax.random.normal(ks[0], (N, L, E), dtype=jnp.float32), 'Wq': jax.random.normal(ks[1], (H, E), dtype=jnp.float32) * s_in, 'bq': jnp.zeros((H,), dtype=jnp.float32), 'Wk': jax.random.normal(ks[2], (H, E), dtype=jnp.float32) * s_in, 'bk': jnp.zeros((H,), dtype=jnp.float32), 'Wv': jax.random.normal(ks[3], (H, E), dtype=jnp.float32) * s_in, 'bv': jnp.zeros((H,), dtype=jnp.float32)}
    _L0_attn_in = _L0_attn_setup()

    def _L0_ffn_setup():
        import jax, jax.numpy as jnp
        import numpy as np
        DIM = 128
        DEPTH = 2
        HEADS = 8
        DIM_HEAD = 64
        WINDOW = 64
        INNER = HEADS * DIM_HEAD
        HID = int(DIM * 4 * 2 / 3)
        B, N = (2, 1024)
        QK_SCALE = 8.0

        def shift_token(t):
            t1, t2 = jnp.split(t, 2, axis=-1)
            t2 = jnp.pad(t2, ((0, 0), (1, 0), (0, 0)))[:, :-1]
            return jnp.concatenate([t1, t2], axis=-1)

        def l2norm(t):
            return t / jnp.clip(jnp.linalg.norm(t, axis=-1, keepdims=True), 1e-12)

        def rotate_half(x):
            x1, x2 = jnp.split(x, 2, axis=-1)
            return jnp.concatenate([-x2, x1], axis=-1)

        def rotary_xpos(q, k):
            n = q.shape[-2]
            half_idx = jnp.arange(0, DIM_HEAD, 2, dtype=jnp.float32)
            inv_freq = 1.0 / 10000.0 ** (half_idx / DIM_HEAD)
            t = jnp.arange(n, dtype=jnp.float32)
            freqs = t[:, None] * inv_freq[None, :]
            freqs = jnp.concatenate([freqs, freqs], axis=-1)
            base = (half_idx + 0.4 * DIM_HEAD) / (1.4 * DIM_HEAD)
            power = (t - n // 2) / float(WINDOW // 2)
            scale = base[None, :] ** power[:, None]
            scale = jnp.concatenate([scale, scale], axis=-1)
            cos, sin = (jnp.cos(freqs), jnp.sin(freqs))
            q = q * cos * scale + rotate_half(q) * sin * scale
            k = k * cos / scale + rotate_half(k) * sin / scale
            return (q, k)

        def local_attention(q, k, v):
            b, h, n, d = q.shape
            w = n // WINDOW
            bq = q.reshape(b, h, w, WINDOW, d) * QK_SCALE
            bk = k.reshape(b, h, w, WINDOW, d)
            bv = v.reshape(b, h, w, WINDOW, d)

            def look_around(t):
                p = jnp.pad(t, ((0, 0), (0, 0), (1, 0), (0, 0), (0, 0)))
                return jnp.concatenate([p[:, :, :w], p[:, :, 1:]], axis=3)
            bk, bv = (look_around(bk), look_around(bv))
            bt = jnp.arange(n).reshape(w, WINDOW)
            btp = jnp.pad(bt, ((1, 0), (0, 0)), constant_values=-1)
            btk = jnp.concatenate([btp[:w], btp[1:]], axis=1)
            sim = jnp.einsum('bhwid,bhwjd->bhwij', bq, bk)
            i = bt[:, :, None]
            j = btk[:, None, :]
            mask = (i < j) | (i > j + WINDOW) | (j == -1)
            sim = jnp.where(mask, -jnp.finfo(sim.dtype).max, sim)
            attn = jax.nn.softmax(sim, axis=-1)
            out = jnp.einsum('bhwij,bhwjd->bhwid', attn, bv)
            return out.reshape(b, h, n, d)

        def _layer(x, wqkv, qs, ksc, wo, lg, lb, w1, b1, w2, b2):
            b, n, _ = x.shape
            h = shift_token(x)
            qkv = h @ wqkv
            q, k, v = jnp.split(qkv, 3, axis=-1)
            to_heads = lambda t: t.reshape(b, n, HEADS, DIM_HEAD).transpose(0, 2, 1, 3)
            q, k, v = (to_heads(q), to_heads(k), to_heads(v))
            q = l2norm(q) * qs
            k = l2norm(k) * ksc
            q, k = rotary_xpos(q, k)
            o = local_attention(q, k, v)
            o = o.transpose(0, 2, 1, 3).reshape(b, n, INNER)
            x = x + o @ wo
            h = shift_token(x)
            mu = h.mean(-1, keepdims=True)
            var = h.var(-1, keepdims=True)
            h = (h - mu) / jnp.sqrt(var + 1e-05) * lg + lb
            h = h @ w1 + b1
            a, g = jnp.split(h, 2, axis=-1)
            h = a * jax.nn.gelu(g, approximate=False)
            x = x + h @ w2 + b2
            return x
        key = jax.random.key(seed)
        ks = jax.random.split(key, 6)
        return {'x': jax.random.normal(ks[0], (B, N, DIM), jnp.float32), 'wqkv': jax.random.normal(ks[1], (DEPTH, DIM, 3 * INNER), jnp.float32) * 0.02, 'q_scale': jnp.ones((DEPTH, DIM_HEAD), jnp.float32), 'k_scale': jnp.ones((DEPTH, DIM_HEAD), jnp.float32), 'wo': jax.random.normal(ks[2], (DEPTH, INNER, DIM), jnp.float32) * 0.02, 'ln_g': jnp.ones((DEPTH, DIM), jnp.float32), 'ln_b': jnp.zeros((DEPTH, DIM), jnp.float32), 'w1': jax.random.normal(ks[3], (DEPTH, DIM, 2 * HID), jnp.float32) * 0.02, 'b1': jnp.zeros((DEPTH, 2 * HID), jnp.float32), 'w2': jax.random.normal(ks[4], (DEPTH, HID, DIM), jnp.float32) * 0.02, 'b2': jnp.zeros((DEPTH, DIM), jnp.float32)}
    _L0_ffn_in = _L0_ffn_setup()

    def _L1_attn_setup():
        import jax, jax.numpy as jnp
        import numpy as np
        D_MODEL = 128
        NUM_HEADS = 16
        D_H = D_MODEL // NUM_HEADS
        BATCH, SEQ = (4, 256)
        key = jax.random.key(seed)
        kx, kq, kk, kv, ko = jax.random.split(key, 5)
        sigma = (2.0 / (D_MODEL + D_MODEL)) ** 0.5

        def trunc(k):
            return jax.random.truncated_normal(k, -3.0, 3.0, (D_MODEL, D_MODEL), dtype=jnp.float32) * sigma
        return {'x': jax.random.normal(kx, (BATCH, SEQ, D_MODEL), dtype=jnp.float32), 'Wq': trunc(kq), 'Wk': trunc(kk), 'Wv': trunc(kv), 'Wo': trunc(ko)}
    _L1_attn_in = _L1_attn_setup()

    def _L1_ffn_setup():
        import jax, jax.numpy as jnp
        import numpy as np
        B, S, H = (4, 256, 128)
        D = 256
        E = 8
        K = 2
        key = jax.random.key(seed)
        ks = jax.random.split(key, 8)
        w = lambda k, shape: jax.random.normal(k, shape, jnp.float32) * 0.02
        return {'hidden_states': jax.random.normal(ks[0], (B, S, H), jnp.float32), 'gate_w': w(ks[1], (H, E)), 'w_gate': w(ks[2], (E, H, D)), 'w_up': w(ks[3], (E, H, D)), 'w_down': w(ks[4], (E, D, H)), 'ws_gate': w(ks[5], (H, D)), 'ws_up': w(ks[6], (H, D)), 'ws_down': w(ks[7], (D, H))}
    _L1_ffn_in = _L1_ffn_setup()
    _d = {'L0_attn_X_embed': _L0_attn_in['X_embed'], 'L0_attn_Wq': _L0_attn_in['Wq'], 'L0_attn_bq': _L0_attn_in['bq'], 'L0_attn_Wk': _L0_attn_in['Wk'], 'L0_attn_bk': _L0_attn_in['bk'], 'L0_attn_Wv': _L0_attn_in['Wv'], 'L0_attn_bv': _L0_attn_in['bv'], 'L0_ffn_wqkv': _L0_ffn_in['wqkv'], 'L0_ffn_q_scale': _L0_ffn_in['q_scale'], 'L0_ffn_k_scale': _L0_ffn_in['k_scale'], 'L0_ffn_wo': _L0_ffn_in['wo'], 'L0_ffn_ln_g': _L0_ffn_in['ln_g'], 'L0_ffn_ln_b': _L0_ffn_in['ln_b'], 'L0_ffn_w1': _L0_ffn_in['w1'], 'L0_ffn_b1': _L0_ffn_in['b1'], 'L0_ffn_w2': _L0_ffn_in['w2'], 'L0_ffn_b2': _L0_ffn_in['b2'], 'L1_attn_Wq': _L1_attn_in['Wq'], 'L1_attn_Wk': _L1_attn_in['Wk'], 'L1_attn_Wv': _L1_attn_in['Wv'], 'L1_attn_Wo': _L1_attn_in['Wo'], 'L1_ffn_gate_w': _L1_ffn_in['gate_w'], 'L1_ffn_w_gate': _L1_ffn_in['w_gate'], 'L1_ffn_w_up': _L1_ffn_in['w_up'], 'L1_ffn_w_down': _L1_ffn_in['w_down'], 'L1_ffn_ws_gate': _L1_ffn_in['ws_gate'], 'L1_ffn_ws_up': _L1_ffn_in['ws_up'], 'L1_ffn_ws_down': _L1_ffn_in['ws_down']}
    _x0 = _d['L0_attn_X_embed']
    _d['L0_attn_X_embed'] = jax.random.normal(jax.random.fold_in(jax.random.key(seed), 1), (8, 512, 128), dtype=_x0.dtype)
    del _x0
    return _d

def reference(L0_attn_X_embed, L0_attn_Wq, L0_attn_bq, L0_attn_Wk, L0_attn_bk, L0_attn_Wv, L0_attn_bv, L0_ffn_wqkv, L0_ffn_q_scale, L0_ffn_k_scale, L0_ffn_wo, L0_ffn_ln_g, L0_ffn_ln_b, L0_ffn_w1, L0_ffn_b1, L0_ffn_w2, L0_ffn_b2, L1_attn_Wq, L1_attn_Wk, L1_attn_Wv, L1_attn_Wo, L1_ffn_gate_w, L1_ffn_w_gate, L1_ffn_w_up, L1_ffn_w_down, L1_ffn_ws_gate, L1_ffn_ws_up, L1_ffn_ws_down):

    def _L0_attn_ref(X_embed, Wq, bq, Wk, bk, Wv, bv):
        import jax, jax.numpy as jnp
        import numpy as np
        N, L, E, H = (4, 512, 128, 128)
        Q = jnp.einsum('nle,he->nlh', X_embed, Wq) + bq
        K = jnp.einsum('nle,he->nlh', X_embed, Wk) + bk
        V = jnp.einsum('nle,he->nlh', X_embed, Wv) + bv
        S = jnp.einsum('nah,nbh->nab', Q, K) / jnp.asarray(np.sqrt(float(L)), dtype=Q.dtype)
        A = jax.nn.softmax(S, axis=1)
        diag = jnp.diagonal(A, axis1=1, axis2=2)
        return diag[:, :, None] * V

    def _L0_ffn_ref(x, wqkv, q_scale, k_scale, wo, ln_g, ln_b, w1, b1, w2, b2):
        import jax, jax.numpy as jnp
        import numpy as np
        DIM = 128
        DEPTH = 2
        HEADS = 8
        DIM_HEAD = 64
        WINDOW = 64
        INNER = HEADS * DIM_HEAD
        HID = int(DIM * 4 * 2 / 3)
        B, N = (2, 1024)
        QK_SCALE = 8.0

        def shift_token(t):
            t1, t2 = jnp.split(t, 2, axis=-1)
            t2 = jnp.pad(t2, ((0, 0), (1, 0), (0, 0)))[:, :-1]
            return jnp.concatenate([t1, t2], axis=-1)

        def l2norm(t):
            return t / jnp.clip(jnp.linalg.norm(t, axis=-1, keepdims=True), 1e-12)

        def rotate_half(x):
            x1, x2 = jnp.split(x, 2, axis=-1)
            return jnp.concatenate([-x2, x1], axis=-1)

        def rotary_xpos(q, k):
            n = q.shape[-2]
            half_idx = jnp.arange(0, DIM_HEAD, 2, dtype=jnp.float32)
            inv_freq = 1.0 / 10000.0 ** (half_idx / DIM_HEAD)
            t = jnp.arange(n, dtype=jnp.float32)
            freqs = t[:, None] * inv_freq[None, :]
            freqs = jnp.concatenate([freqs, freqs], axis=-1)
            base = (half_idx + 0.4 * DIM_HEAD) / (1.4 * DIM_HEAD)
            power = (t - n // 2) / float(WINDOW // 2)
            scale = base[None, :] ** power[:, None]
            scale = jnp.concatenate([scale, scale], axis=-1)
            cos, sin = (jnp.cos(freqs), jnp.sin(freqs))
            q = q * cos * scale + rotate_half(q) * sin * scale
            k = k * cos / scale + rotate_half(k) * sin / scale
            return (q, k)

        def local_attention(q, k, v):
            b, h, n, d = q.shape
            w = n // WINDOW
            bq = q.reshape(b, h, w, WINDOW, d) * QK_SCALE
            bk = k.reshape(b, h, w, WINDOW, d)
            bv = v.reshape(b, h, w, WINDOW, d)

            def look_around(t):
                p = jnp.pad(t, ((0, 0), (0, 0), (1, 0), (0, 0), (0, 0)))
                return jnp.concatenate([p[:, :, :w], p[:, :, 1:]], axis=3)
            bk, bv = (look_around(bk), look_around(bv))
            bt = jnp.arange(n).reshape(w, WINDOW)
            btp = jnp.pad(bt, ((1, 0), (0, 0)), constant_values=-1)
            btk = jnp.concatenate([btp[:w], btp[1:]], axis=1)
            sim = jnp.einsum('bhwid,bhwjd->bhwij', bq, bk)
            i = bt[:, :, None]
            j = btk[:, None, :]
            mask = (i < j) | (i > j + WINDOW) | (j == -1)
            sim = jnp.where(mask, -jnp.finfo(sim.dtype).max, sim)
            attn = jax.nn.softmax(sim, axis=-1)
            out = jnp.einsum('bhwij,bhwjd->bhwid', attn, bv)
            return out.reshape(b, h, n, d)

        def _layer(x, wqkv, qs, ksc, wo, lg, lb, w1, b1, w2, b2):
            b, n, _ = x.shape
            h = shift_token(x)
            qkv = h @ wqkv
            q, k, v = jnp.split(qkv, 3, axis=-1)
            to_heads = lambda t: t.reshape(b, n, HEADS, DIM_HEAD).transpose(0, 2, 1, 3)
            q, k, v = (to_heads(q), to_heads(k), to_heads(v))
            q = l2norm(q) * qs
            k = l2norm(k) * ksc
            q, k = rotary_xpos(q, k)
            o = local_attention(q, k, v)
            o = o.transpose(0, 2, 1, 3).reshape(b, n, INNER)
            x = x + o @ wo
            h = shift_token(x)
            mu = h.mean(-1, keepdims=True)
            var = h.var(-1, keepdims=True)
            h = (h - mu) / jnp.sqrt(var + 1e-05) * lg + lb
            h = h @ w1 + b1
            a, g = jnp.split(h, 2, axis=-1)
            h = a * jax.nn.gelu(g, approximate=False)
            x = x + h @ w2 + b2
            return x
        for l in range(DEPTH):
            x = _layer(x, wqkv[l], q_scale[l], k_scale[l], wo[l], ln_g[l], ln_b[l], w1[l], b1[l], w2[l], b2[l])
        return x

    def _L1_attn_ref(x, Wq, Wk, Wv, Wo):
        import jax, jax.numpy as jnp
        import numpy as np
        D_MODEL = 128
        NUM_HEADS = 16
        D_H = D_MODEL // NUM_HEADS
        BATCH, SEQ = (4, 256)
        B, S, D = x.shape
        H, Dh = (NUM_HEADS, D_H)
        q = jnp.einsum('oi,bsi->bso', Wq, x)
        k = jnp.einsum('oi,bsi->bso', Wk, x)
        v = jnp.einsum('oi,bsi->bso', Wv, x)
        q = q.reshape(B, S, H, Dh).transpose(0, 2, 1, 3)
        k = k.reshape(B, S, H, Dh).transpose(0, 2, 1, 3)
        v = v.reshape(B, S, H, Dh).transpose(0, 2, 1, 3)
        scale = 1.0 / jnp.sqrt(jnp.asarray(Dh, dtype=x.dtype))
        score = jnp.einsum('bhnd,bhmd->bhnm', q, k) * scale
        causal = jnp.tril(jnp.ones((S, S), dtype=bool))
        score = jnp.where(causal, score, -jnp.inf)
        attn = jax.nn.softmax(score, axis=-1)
        out = jnp.einsum('bhnm,bhmd->bhnd', attn, v)
        out = out.transpose(0, 2, 1, 3).reshape(B, S, D)
        return jnp.einsum('oi,bsi->bso', Wo, out)

    def _L1_ffn_ref(hidden_states, gate_w, w_gate, w_up, w_down, ws_gate, ws_up, ws_down):
        import jax, jax.numpy as jnp
        import numpy as np
        B, S, H = (4, 256, 128)
        D = 256
        E = 8
        K = 2
        b, s, h = hidden_states.shape
        x = hidden_states.reshape(-1, h)
        scores = jax.nn.softmax(x @ gate_w, axis=-1)
        topk_w, topk_idx = jax.lax.top_k(scores, K)
        topk_w = topk_w / (jnp.sum(topk_w, axis=-1, keepdims=True) + 1e-20)
        onehot = jax.nn.one_hot(topk_idx, E, dtype=x.dtype)
        w_per_expert = jnp.einsum('nke,nk->ne', onehot, topk_w)
        y = jnp.zeros_like(x)
        for e in range(E):
            hid = jax.nn.silu(x @ w_gate[e]) * (x @ w_up[e])
            y = y + w_per_expert[:, e:e + 1] * (hid @ w_down[e])
        shared = jax.nn.silu(x @ ws_gate) * (x @ ws_up) @ ws_down
        return (y + shared).reshape(b, s, h)
    x = L0_attn_X_embed
    x = x + _L0_attn_ref(_layernorm(x, axis=-1), L0_attn_Wq, L0_attn_bq, L0_attn_Wk, L0_attn_bk, L0_attn_Wv, L0_attn_bv)
    x = x + _L0_ffn_ref(_layernorm(x, axis=-1), L0_ffn_wqkv, L0_ffn_q_scale, L0_ffn_k_scale, L0_ffn_wo, L0_ffn_ln_g, L0_ffn_ln_b, L0_ffn_w1, L0_ffn_b1, L0_ffn_w2, L0_ffn_b2)
    x = x + _L1_attn_ref(_layernorm(x, axis=-1), L1_attn_Wq, L1_attn_Wk, L1_attn_Wv, L1_attn_Wo)
    x = x + _L1_ffn_ref(_layernorm(x, axis=-1), L1_ffn_gate_w, L1_ffn_w_gate, L1_ffn_w_up, L1_ffn_w_down, L1_ffn_ws_gate, L1_ffn_ws_up, L1_ffn_ws_down)
    return x

_drawn_inputs = setup_inputs


def setup_inputs(seed=0):
    import zlib

    import numpy as np

    out = dict(_drawn_inputs(seed))
    spreads = {'L0_attn_bq': (0.0, 2.0),
     'L0_attn_bk': (0.0, 2.0),
     'L0_attn_bv': (0.0, 2.0),
     'L0_ffn_q_scale': (1.0, 0.6),
     'L0_ffn_k_scale': (1.0, 0.6),
     'L0_ffn_ln_g': (1.0, 0.6),
     'L0_ffn_ln_b': (0.0, 0.8),
     'L0_ffn_b1': (0.0, 0.8),
     'L0_ffn_b2': (0.0, 0.1)}
    factors = {'L0_attn_Wq': 8.0,
     'L0_attn_Wk': 8.0,
     'L0_attn_Wv': 8.0,
     'L0_ffn_wqkv': 3.518,
     'L0_ffn_wo': 3.546,
     'L0_ffn_w1': 6.12,
     'L0_ffn_w2': 6.021,
     'L1_ffn_gate_w': 8.0,
     'L1_ffn_w_gate': 8.0,
     'L1_ffn_w_up': 8.0,
     'L1_ffn_w_down': 8.0,
     'L1_ffn_ws_gate': 8.0,
     'L1_ffn_ws_up': 8.0,
     'L1_ffn_ws_down': 8.0,
     'L1_attn_Wq': 3.143,
     'L1_attn_Wk': 3.195}
    for name, (base, spread) in spreads.items():
        noise = np.random.default_rng([zlib.crc32(name.encode()), seed]).standard_normal(out[name].shape)
        drawn = base * np.exp(spread * noise) if base else spread * noise
        out[name] = jnp.asarray(drawn.astype(out[name].dtype))
    for name, factor in factors.items():
        out[name] = (out[name] * factor).astype(out[name].dtype)
    return out
```

```python
from contextlib import ExitStack

import numpy as np

import concourse.bass as bass
from concourse import mybir
from concourse.alu_op_type import AluOpType as ALU

ACT = mybir.ActivationFunctionType
AX = mybir.AxisListType
F32 = mybir.dt.float32
BF16 = mybir.dt.bfloat16
U32 = mybir.dt.uint32

P = 128
SEQS, T = 8, 512
NT = T // P
LAYERS = 2
HEADS, DH = 8, 64
WINDOW = 64
NW = T // WINDOW
INNER = HEADS * DH
NP = INNER // P
HID = 341
HC, HT = 3, 114
CH, CD = 16, 8
RH = 8
EXPERTS, MH = 8, 256
ALL = EXPERTS + 1
SLOTS = 3
NEG = -(2.0 ** 100)
EPS = 1e-5
ROWS_QK, ROWS_ALL = 96, 128

FRONT = [("ln", 0), ("tp", 1), ("qkv", 3), ("scores", 4), ("tp2", 1)] + [
    (f"{n}{l}", w) for l in range(LAYERS) for n, w in (
        ("qkv01", 5), ("qkv23", 5), ("turn01", 1), ("turn23", 1), ("sim0", 5), ("sim1", 5),
        ("pt0", 2), ("pt1", 4), ("pv1", 4), ("wo", 3), ("mean", 1), ("var", 1), ("w1", 5), ("w2", 3))
] + [("out", 1)]
BACK = [("ln", 0), ("tp", 1), ("qkv", 3)] + [
    (f"{n}{r}", w) for r in range(2) for n, w in (
        ("pack", 0), ("max0", 3), ("max1", 3), ("maxT", 1), ("s0", 3), ("s1pv0", 5), ("pv1", 2))
] + [("turn", 2), ("otp", 1), ("wo", 1), ("ln2", 1), ("route", 1)] + [
    (f"moe{e}", 5) for e in range(ALL)] + [("last", 2)]


ORDER = "BBFBFFFBBFBFFBBFBFBFFFBBBFBFFFBFBFBFBFBFBFBBBFBFBFFBFFBFBFBBFBFFBF"


def merged():
    assert ORDER.count("F") == len(FRONT) and ORDER.count("B") == len(BACK)
    return ["FB".index(half) for half in ORDER]


MAX_FILLS = [(0, [0, 1, 2, 3]), (0, [4, 5, 6, 7])] + [(1, [h, h + 1]) for h in range(0, RH, 2)] + \
    [(t, [h]) for t in (2, 3) for h in range(RH)]
EXP_FILLS = [f for a in (0, 2) for f in ([(a, 0)], [(a + 1, 0)], [(a, 1), (a, 3)], [(a + 1, 1), (a + 1, 3)],
                                         [(a, 2), (a + 1, 2)])]


def exp_places():
    out = {}
    for n, fill in enumerate(EXP_FILLS):
        at = 0
        for hd, kk in fill:
            out[(hd, kk)] = (n, at)
            at += T - kk * P
    return out


EXP_AT = exp_places()


def run_halves(engine, front, back):
    assert sum(1 for _ in front(0)) == len(FRONT)
    with engine.Fori(0, SEQS - 1) as t:
        halves = [front(t + 1), back(t)]
        for half in merged():
            next(halves[half])
        for half in halves:
            assert next(half, None) is None and next(half, 0) == 0
    assert sum(1 for _ in back(SEQS - 1, last=True)) == len(BACK)


class Signal:

    def __init__(self, nc, ctx, name, per, unit=1):
        self.sem, self.name, self.per, self.unit = ctx.enter_context(nc.semaphore(name)), name, per, unit

    def at(self, s, k):
        assert 1 <= k <= self.per, (self.name, k)
        return (s * self.per + k) * self.unit


class Chain(Signal):

    def start(self):
        self.k = 0

    def one(self):
        self.k += 1
        return 1

    def now(self, s):
        return self.at(s, self.k)


def finish(chain):
    assert chain.k == chain.per, f"{chain.name} {chain.k} != {chain.per}"


def program(nc, io, out):
    ctx = ExitStack()
    with ctx:
        def sb(name, shape, dt=F32):
            return ctx.enter_context(nc.sbuf_tensor(name, shape, dt))

        def sig(name, per, unit=1):
            return Signal(nc, ctx, name, per, unit)

        def chain(name, per):
            return Chain(nc, ctx, name, per)

        aw = sb("aw", [P, 3, P])
        ab = sb("ab", [P, 3])
        abq = sb("abq", [P, 1])
        abv = sb("abv", [P, P])
        wqkv = sb("wqkv", [P, LAYERS, 3 * INNER])
        wo = sb("wo", [P, LAYERS, NP, P])
        w1 = sb("w1", [P, LAYERS, 2, HC, HT])
        w2 = sb("w2", [HT, LAYERS, HC, P])
        b1 = sb("b1", [HT, LAYERS, 2, HC])
        b2 = sb("b2", [P, LAYERS])
        lng = sb("lng", [P, LAYERS])
        lnb = sb("lnb", [P, LAYERS])
        qks = sb("qks", [P, LAYERS, 2, DH])
        cosT = sb("cosT", [P, LAYERS, NT, 2, DH])
        sinT = sb("sinT", [P, LAYERS, NT, 2, DH])
        cw = sb("cw", [P, 4, P])
        gw = sb("gw", [P, EXPERTS])
        mw = sb("mw", [P, SLOTS, 3 * MH])
        ident = sb("ident", [P, P])
        identb = sb("identb", [P, P], BF16)
        mean_w = sb("mean_w", [P, P])
        maskb = sb("maskb", [P, 2 * T + 2 * P], BF16)
        iota = sb("iota", [P, EXPERTS])
        pause = sb("pause", [P, 1])
        consts = sb("consts", [P, 2])
        local_mask = [maskb[:, 0:T], maskb[:, T:2 * T]]
        causal_qk, causal_kq = maskb[:, 2 * T:2 * T + P], maskb[:, 2 * T + P:2 * T + 2 * P]

        xin = sb("xin", [P, NT, P])
        x1 = sb("x1", [P, NT, P])
        fxn = sb("fxn", [P, NT, P])
        fst = sb("fst", [P, NT, 6])
        fmv = sb("fmv", [P, NT, 2])
        frs = sb("frs", [P, 2, NT])
        h = sb("h", [P, T + 4])
        hs = h[:, 0:T]
        work1 = sb("work1", [P, 4096])
        work2 = sb("work2", [P, 4096])
        qt = sb("qt", [P, NP, T])
        kt = sb("kt", [P, NP, 2, WINDOW + T])
        v = sb("v", [P, NT, INNER])
        v2 = sb("v2", [P, NT, INNER])
        small = sb("small", [P, 8 * NP * NP + 64])
        x2 = sb("x2", [P, NT, P])

        axt = qt[:, 0, :]
        aqt, akt = qt[:, 1, :], qt[:, 2, :]
        av = v[:, 0, :].rearrange("p (a b) -> p a b", a=NT)
        ae = work1[:, 0:NT * T].rearrange("p (a b) -> p a b", a=NT)
        aed = work1[:, 0:NT * (T + P)].rearrange("p (a b) -> p a b", a=NT)[:, :, 0:P]
        adj = work2[:, 0:NT * P].rearrange("p (a b) -> p a b", a=NT)
        am, asum, adiag, arec = (small[:, 4 * i:4 * i + 4] for i in range(4))

        qk = work1[:, :].rearrange("p (a b) -> p a b", a=NT)
        part = [work2[:, 1024 * i:1024 * (i + 1)] for i in range(2)]
        sq = work2[:, 2048:3072]
        ss = small[:, 16:80].rearrange("p (a b) -> p a b", a=NT)
        rn = small[:, 80:144].rearrange("p (a b) -> p a b", a=NT)
        pr = work1[:, :].rearrange("p (f a b) -> p f a b", f=2 * NP, b=P)
        pt = work2[:, :].rearrange("p (f a b) -> p f a b", f=2 * NP, b=P)
        pmax = small[:, 0:32]
        psum_ = sb("psums", [P, 32])
        prec = sb("prec", [P, 32])
        hg = work1[0:HT, 0:HC * T].rearrange("p (a b) -> p a b", a=HC)
        gel = [work1[0:HT, HC * T + i * T:HC * T + (i + 1) * T] for i in range(2)]
        dc, dsq, drs = (work1[:, (5 + i) * T:(6 + i) * T] for i in range(3))
        cs_in = work1[:, 0:2 * NT * 2 * DH].rearrange("p (z a j d) -> p z a j d", z=2, a=NT, j=2)
        maskf = work2[:, 0:2 * T + 2 * P]
        hn = work2[:, 0:T]
        fin = work2[:, T:2 * T]

        bxn = sb("bxn", [P, NT, P])
        bst = sb("bst", [P, NT, 6])
        bmv = sb("bmv", [P, NT, 2])
        brs = sb("brs", [P, 2, NT])
        bxt = sb("bxt", [P, T])
        x3 = sb("x3", [P, NT, P])
        pq = sb("pq", [P, RH, T], BF16)
        pk = sb("pk", [P, RH, T], BF16)
        va = sb("va", [P, NT, CH, 32])
        ctmp = sb("ctmp", [P, 4, T])
        big = sb("big", [P, 10, T])
        cmax = sb("cmax", [P, 2, RH, NT])
        mrow = sb("mrow", [RH * NT, 3, P], BF16)
        mrem = sb("mrem", [RH * NT, 2, P])
        outb = x3
        qkf, qkr = ctmp[:, 0:2, :], ctmp[:, 2:4, :]
        oc = ctmp
        parts = big[:, 0:3, :].bitcast(BF16).rearrange("p a (b c) -> p a b c", b=2)
        on = bxn
        ont = bxt
        crec = sb("crec", [P, CH])
        silu = [big[:, 2 * i:2 * i + 2, :] for i in range(2)]
        hid = [big[:, 4 + 2 * i:6 + 2 * i, :] for i in range(2)]
        rt = sb("rt", [P, 8, NT, EXPERTS])
        rti = sb("rti", [P, NT, EXPERTS], U32)
        rs1 = sb("rs1", [P, 4, NT])
        gate = sb("gate", [P, NT, EXPERTS])

        ps = [ctx.enter_context(nc.psum_tensor(f"ps{i}", [P, T], F32))[:, :] for i in range(8)]
        fb, bb = ps[0:4], ps[4:8]

        scr = nc.dram_tensor("scr_parts", [3, 2, CH, CD, T], BF16).ap()
        scrm = nc.dram_tensor("scr_max", [3, RH * NT, P], BF16).ap()

        loaded = ctx.enter_context(nc.semaphore("constants_loaded"))
        ready_v = ctx.enter_context(nc.semaphore("vector_constants_ready"))
        ready_p = ctx.enter_context(nc.semaphore("gpsimd_constants_ready"))
        x3_free = ctx.enter_context(nc.semaphore("x3_free"))

        s_x = sig("x_loaded", 1, 16)
        f_stats, f_rstd, f_xn, f_tp, f_xt = (sig(n, 2) for n in ("f_stats", "f_rstd", "f_xn", "f_turned", "f_xt"))
        a_qkv, a_qk, a_v = sig("a_qkv", 3), sig("a_qk", 2), sig("a_v", 1)
        a_s, a_max, a_e, a_x1 = sig("a_scores", 4), sig("a_max", 4), sig("a_exp", 4), sig("a_x1", 1)
        l_qkv = sig("l_qkv", LAYERS * 12)
        l_ev = sig("l_qkv_evacuated", LAYERS * 12)
        l_sq, l_ss = sig("l_squares", LAYERS * 4), sig("l_square_sums", LAYERS * 4)
        l_rot, l_add = sig("l_rotary_products", LAYERS * 4), sig("l_rotary_sum", LAYERS * 4)
        l_ssc, l_rn, l_qkn = sig("l_norms_guarded", LAYERS), sig("l_inverse_norms", LAYERS), sig("l_normalised", LAYERS * 4)
        l_v2 = sig("l_v_shifted", LAYERS * 2, 16)
        l_tq, l_tk = sig("l_q_turned", LAYERS * 4), sig("l_k_turned", LAYERS * 4)
        l_qt, l_kt = sig("l_qt", LAYERS * 4), sig("l_kt", LAYERS * 4)
        l_sim, l_max, l_exp = sig("l_sims", LAYERS * 8), sig("l_max", LAYERS * 8), sig("l_exp", LAYERS * 8)
        l_rec, l_pn = sig("l_sum_inverse", LAYERS * 8), sig("l_probs", LAYERS * 8)
        l_pt, l_ptv, l_pta = sig("l_probs_turned", LAYERS * 8), sig("l_pt_dve", LAYERS * 4), sig("l_pt_act", LAYERS * 4)
        l_pv, l_ot = sig("l_pv", LAYERS * 4), sig("l_ot", LAYERS * 4)
        l_wo, l_h1 = sig("l_wo", LAYERS), sig("l_h1", LAYERS)
        l_mean, l_dc, l_dsq, l_var = sig("l_mean", LAYERS), sig("l_centred", LAYERS), sig("l_centred_sq", LAYERS), sig("l_var", LAYERS)
        l_drs, l_dn, l_hn = sig("l_rstd", LAYERS), sig("l_dn", LAYERS), sig("l_hn", LAYERS)
        l_g, l_a, l_gelu, l_hg = sig("l_g", LAYERS * 3), sig("l_a", LAYERS * 3), sig("l_gelu", LAYERS * 3), sig("l_hg", LAYERS * 3)
        l_w2, l_h2 = sig("l_w2", LAYERS), sig("l_h2", LAYERS)
        f_ft, f_x2 = sig("f_out_turned", 1), sig("f_x2", 1)
        fv, fa = chain("front_vector", 14), chain("front_scalar", 6)

        b_stats, b_rstd, b_xn, b_tp, b_xt = (sig(n, 2) for n in ("b_stats", "b_rstd", "b_xn", "b_turned", "b_xt"))
        c_qkv, c_qkf, c_v = sig("c_qkv", 3), sig("c_qkf", 2), sig("c_v", 1)
        c_parts, c_saved = sig("c_parts", 1), sig("c_parts_saved", 1, 16)
        c_packed = sig("c_packed", 2 * 18, 16)
        c_s1, c_m = sig("c_max_scores", 2 * 22), sig("c_row_max", 2 * 22)
        c_mt, c_mr = sig("c_max_turned", 2), sig("c_max_parts", 2)
        c_msaved, c_mpacked = sig("c_max_saved", 2, 16), sig("c_max_packed", 2, 16)
        c_s2, c_e = sig("c_scores", 4 * 10), sig("c_exp", 4 * 10)
        c_pv, c_oc = sig("c_pv", 4), sig("c_oc", 4)
        c_ot, c_on = sig("c_out_turned", 4), sig("c_out_norm", 4)
        c_ont, c_onx, c_wo, c_x3 = sig("c_on_turned", 1), sig("c_ont", 1), sig("c_wo", 1), sig("c_x3", 1)
        r_l, r_m, r_e, r_w = sig("r_logits", 1), sig("r_centred", 1), sig("r_exp", 1), sig("r_gates", 1)
        m_g, m_u, m_d = sig("m_gate", ALL * 2), sig("m_up", ALL * 2), sig("m_down", ALL)
        m_silu, m_hid, m_sum = sig("m_silu", ALL * 2), sig("m_hidden", ALL * 2), sig("m_sum", ALL)
        s_mw = [sig(f"expert_loaded{i}", ALL // SLOTS, 16) for i in range(SLOTS)]
        bv, ba = chain("back_vector", 30), chain("back_scalar", 2)

        block = ctx.enter_context(nc.Block())
        loads = [
            (aw[:, :, :], io["aw"]), (ab[:, :], io["ab"]), (abv[:, :], io["abv"].unsqueeze(0).broadcast_to([P, P])),
            (wqkv[:, :, :], io["wqkv"].rearrange("l p n -> p l n")), (wo[:, :, :, :], io["wo"].rearrange("l (c p) n -> p l c n", p=P)),
            (w1[:, :, :, :, :], io["w1"]), (w2[:, :, :, :], io["w2"]), (b1[:, :, :, :], io["b1"]), (b2[:, :], io["b2"]),
            (lng[:, :], io["ln_g"]), (lnb[:, :], io["ln_b"]), (cw[:, :, :], io["cw"]), (gw[:, :], io["gate_w"]),
            (ident[:, :], io["ident"]), (maskf, io["masks"]), (cs_in, io["rotary"]), (iota[:, :], io["iota"]),
        ]
        n_loads = len(loads)

        @block.tensor
        def _(pe):
            pe.wait_ge(loaded, 16 * n_loads)
            pe.wait_ge(ready_v, 1)
            pe.wait_ge(ready_p, 2)

            def mm(o, a, b, start=True, stop=True):
                return nc.tensor.matmul(o, a, b, start=start, stop=stop, skip_group_check=True)

            def turn_tiles(bank, src):
                for tt in range(NT):
                    i = nc.tensor.transpose(bank[:, tt * P:(tt + 1) * P], src(tt), ident[:, :])
                return i

            def front(s):
                yield
                pe.wait_ge(f_xn.sem, f_xn.at(s, 1))
                turn_tiles(fb[0], lambda tt: fxn[:, tt, :]).then_inc(f_tp.sem, 1)
                yield
                pe.wait_ge(f_xt.sem, f_xt.at(s, 1))
                mm(fb[1], aw[:, 0, :], axt).then_inc(a_qkv.sem, 1)
                mm(fb[2], aw[:, 1, :], axt).then_inc(a_qkv.sem, 1)
                for tt in range(NT):
                    i = mm(fb[3][:, tt * P:(tt + 1) * P], axt[:, tt * P:(tt + 1) * P], aw[:, 2, :])
                i.then_inc(a_qkv.sem, 1)
                yield
                pe.wait_ge(a_qk.sem, a_qk.at(s, 2))
                pe.wait_ge(a_v.sem, a_v.at(s, 1))
                for b in range(NT):
                    mm(fb[b], akt[:, b * P:(b + 1) * P], aqt).then_inc(a_s.sem, 1)
                yield
                pe.wait_ge(f_xn.sem, f_xn.at(s, 2))
                turn_tiles(fb[0], lambda tt: fxn[:, tt, :]).then_inc(f_tp.sem, 1)
                yield
                for l in range(LAYERS):
                    if l == 0:
                        pe.wait_ge(f_xt.sem, f_xt.at(s, 2))
                    else:
                        pe.wait_ge(l_h2.sem, l_h2.at(s, l))
                    for tt in range(NT):
                        for j in range(3):
                            n = 3 * tt + j
                            if n >= 4:
                                pe.wait_ge(l_ev.sem, l_ev.at(s, 12 * l + n - 3))
                            mm(fb[n % 4], hs[:, tt * P:(tt + 1) * P],
                                               wqkv[:, l, j * INNER:(j + 1) * INNER]).then_inc(l_qkv.sem, 1)
                        if tt == 1:
                            yield
                    yield
                    for tt in range(NT):
                        if tt == 0:
                            pe.wait_ge(l_ev.sem, l_ev.at(s, 12 * l + 12))
                        pe.wait_ge(l_qkn.sem, l_qkn.at(s, 4 * l + tt + 1))
                        if tt >= 2:
                            pe.wait_ge(l_qt.sem, l_qt.at(s, 4 * l + tt - 1))
                        turn_tiles(fb[2 * tt % 4], lambda c: qk[:, tt, c * P:(c + 1) * P]).then_inc(l_tq.sem, 1)
                        if tt >= 2:
                            pe.wait_ge(l_kt.sem, l_kt.at(s, 4 * l + tt - 1))
                        turn_tiles(fb[(2 * tt + 1) % 4], lambda c: qk[:, tt, INNER + c * P:INNER + (c + 1) * P]).then_inc(l_tk.sem, 1)
                        if tt == 1:
                            yield
                    yield
                    pe.wait_ge(l_qt.sem, l_qt.at(s, 4 * l + 4))
                    pe.wait_ge(l_kt.sem, l_kt.at(s, 4 * l + 4))
                    for f in range(2 * NP):
                        p, half = divmod(f, 2)
                        if f >= 4:
                            pe.wait_ge(l_exp.sem, l_exp.at(s, 8 * l + f - 3))
                        bank = fb[f % 4]
                        mm(bank, identb[:, :], local_mask[half], stop=False)
                        for w in range(4 * half, 4 * half + 4):
                            par, col = w % 2, (w // 2 % 2) * 2 * P
                            i = mm(bank[64 * par:64 * par + 64, col:col + 2 * P],
                                   qt[:, p, w * WINDOW:(w + 1) * WINDOW],
                                   kt[:, p, :, w * WINDOW:(w + 2) * WINDOW], start=False)
                        i.then_inc(l_sim.sem, 1)
                        if f == 3:
                            yield
                    yield
                    def turn_probs(f):
                        pe.wait_ge(l_pn.sem, l_pn.at(s, 8 * l + f + 1))
                        if f < 4:
                            pe.wait_ge(l_exp.sem, l_exp.at(s, 8 * l + f + 5))
                        elif f % 2 == 0:
                            pe.wait_ge(l_ptv.sem, l_ptv.at(s, 4 * l + (f - 4) // 2 + 1))
                        else:
                            pe.wait_ge(l_pta.sem, l_pta.at(s, 4 * l + (f - 4) // 2 + 1))
                        turn_tiles(fb[f % 4], lambda c: pr[:, f, c, :]).then_inc(l_pt.sem, 1)

                    def pv(p):
                        if p == 0:
                            pe.wait_ge(l_v2.sem, l_v2.at(s, 2 * l + 2))
                        pe.wait_ge(l_ptv.sem, l_ptv.at(s, 4 * l + min(p + 3, 4)))
                        pe.wait_ge(l_pta.sem, l_pta.at(s, 4 * l + min(p + 3, 4)))
                        for a in range(2):
                            for w in range(NW):
                                vt = v[:, w // 2, :] if w % 2 else v2[:, w // 2, :]
                                i = mm(fb[p][64 * a:64 * a + 64, w * WINDOW:(w + 1) * WINDOW],
                                       vt[:, (2 * p + a) * DH:(2 * p + a + 1) * DH],
                                       pt[:, 2 * p + w // 4, 2 * (w // 2 % 2) + a, 64 * (w % 2):64 * (w % 2) + 64])
                        i.then_inc(l_pv.sem, 1)

                    for f in range(4):
                        turn_probs(f)
                    yield
                    for f in range(4, 8):
                        turn_probs(f)
                    pv(0)
                    pv(1)
                    yield
                    pv(2)
                    pv(3)
                    yield
                    pe.wait_ge(l_ot.sem, l_ot.at(s, 4 * l + 4))
                    for p in range(NP):
                        i = mm(fb[0], wo[:, l, p, :], qt[:, p, :], start=(p == 0), stop=(p == NP - 1))
                    i.then_inc(l_wo.sem, 1)
                    yield
                    pe.wait_ge(l_h1.sem, l_h1.at(s, l + 1))
                    mm(fb[1], mean_w[:, :], hs).then_inc(l_mean.sem, 1)
                    yield
                    pe.wait_ge(l_dsq.sem, l_dsq.at(s, l + 1))
                    mm(fb[2], mean_w[:, :], dsq).then_inc(l_var.sem, 1)
                    yield
                    pe.wait_ge(l_hn.sem, l_hn.at(s, l + 1))
                    for c in range(HC):
                        if c == 2:
                            pe.wait_ge(l_gelu.sem, l_gelu.at(s, 3 * l + 1))
                        mm(fb[2 * c % 4][0:HT, :], w1[:, l, 1, c, :], hn).then_inc(l_g.sem, 1)
                        if c == 2:
                            pe.wait_ge(l_hg.sem, l_hg.at(s, 3 * l + 1))
                        mm(fb[(2 * c + 1) % 4][0:HT, :], w1[:, l, 0, c, :], hn).then_inc(l_a.sem, 1)
                    yield
                    pe.wait_ge(l_hg.sem, l_hg.at(s, 3 * l + 3))
                    for c in range(HC):
                        i = mm(fb[2], w2[:, l, c, :], hg[:, c, :], start=(c == 0), stop=(c == HC - 1))
                    i.then_inc(l_w2.sem, 1)
                    yield
                pe.wait_ge(l_h2.sem, l_h2.at(s, LAYERS))
                turn_tiles(fb[3], lambda tt: fin[:, tt * P:(tt + 1) * P]).then_inc(f_ft.sem, 1)
                yield

            def back(s, last=False):
                yield
                pe.wait_ge(b_xn.sem, b_xn.at(s, 1))
                turn_tiles(bb[0], lambda tt: bxn[:, tt, :]).then_inc(b_tp.sem, 1)
                yield
                pe.wait_ge(b_xt.sem, b_xt.at(s, 1))
                mm(bb[1], cw[:, 0, :], bxt[:, :]).then_inc(c_qkv.sem, 1)
                mm(bb[2], cw[:, 1, :], bxt[:, :]).then_inc(c_qkv.sem, 1)
                for tt in range(NT):
                    i = mm(bb[3][:, tt * P:(tt + 1) * P], bxt[:, tt * P:(tt + 1) * P], cw[:, 2, :])
                i.then_inc(c_qkv.sem, 1)
                yield
                for r in range(2):
                    yield
                    pe.wait_ge(c_packed.sem, c_packed.at(s, 18 * (r + 1)))
                    if r == 0:
                        pe.wait_ge(c_qkf.sem, c_qkf.at(s, 2))
                        pe.wait_ge(c_v.sem, c_v.at(s, 1))
                    else:
                        pe.wait_ge(c_e.sem, c_e.at(s, 20))
                        pe.wait_ge(c_oc.sem, c_oc.at(s, 2))
                    for n, (t, heads) in enumerate(MAX_FILLS):
                        if n >= 4:
                            pe.wait_ge(c_m.sem, c_m.at(s, 22 * r + n - 3))
                        for j, hd in enumerate(heads):
                            at, cols = j * (t + 1) * P, (t + 1) * P
                            mm(bb[n % 4][:, at:at + cols], pq[0:ROWS_QK, hd, t * P:(t + 1) * P], pk[0:ROWS_QK, hd, 0:cols],
                               stop=False)
                            i = mm(bb[n % 4][:, at + t * P:at + cols], identb[:, :], causal_qk, start=False)
                        i.then_inc(c_s1.sem, 1)
                        if n == 10:
                            yield
                    yield
                    pe.wait_ge(c_m.sem, c_m.at(s, 22 * (r + 1)))
                    nc.tensor.transpose(bb[0][0:RH * NT, 0:P], cmax[:, r, :, :].rearrange("p a b -> p (a b)"),
                                                       ident[:, :]).then_inc(c_mt.sem, 1)
                    yield

                    def scores(g):
                        if g % 2 == 0:
                            pe.wait_ge(c_mpacked.sem, c_mpacked.at(s, r + 1))
                        for n, fill in enumerate(EXP_FILLS):
                            k = 10 * (2 * r + g) + n
                            if k % 20 >= 3:
                                pe.wait_ge(c_e.sem, c_e.at(s, k - 2))
                            bank = bb[k % 20 % 3]
                            at = 0
                            for hd, kk in fill:
                                hh = 4 * g + hd
                                cols = T - kk * P
                                mm(bank[:, at:at + cols], pk[:, hh, kk * P:(kk + 1) * P], pq[:, hh, kk * P:T], stop=False)
                                i = mm(bank[:, at:at + P], identb[:, :], causal_kq, start=False)
                                at += cols
                            i.then_inc(c_s2.sem, 1)

                    def pv(g):
                        gg = 2 * r + g
                        pe.wait_ge(c_e.sem, c_e.at(s, 10 * (gg + 1)))
                        if g == 1:
                            pe.wait_ge(c_oc.sem, c_oc.at(s, gg))
                        for kk in range(NT):
                            for hd in range(4):
                                slot, at = EXP_AT[(hd, kk)]
                                i = mm(bb[3][32 * hd:32 * hd + 32, kk * P:T], va[:, kk, 4 * gg + hd, :],
                                       big[:, slot, at:at + T - kk * P], start=(kk == 0), stop=(kk == NT - 1))
                        i.then_inc(c_pv.sem, 1)

                    pe.wait_ge(c_mr.sem, c_mr.at(s, r + 1))
                    scores(0)
                    yield
                    pv(0)
                    scores(1)
                    yield
                    pv(1)
                    yield
                pe.wait_ge(c_oc.sem, c_oc.at(s, 4))
                pe.wait_ge(c_e.sem, c_e.at(s, 40))
                for tt in range(NT):
                    for g in range(4):
                        i = nc.tensor.transpose(bb[tt][:, g * P:(g + 1) * P], oc[:, g, tt * P:(tt + 1) * P], ident[:, :])
                    i.then_inc(c_ot.sem, 1)
                yield
                pe.wait_ge(c_on.sem, c_on.at(s, 4))
                turn_tiles(bb[0], lambda tt: on[:, tt, :]).then_inc(c_ont.sem, 1)
                yield
                pe.wait_ge(c_onx.sem, c_onx.at(s, 1))
                for tt in range(NT):
                    i = mm(bb[1][:, tt * P:(tt + 1) * P], ont[:, tt * P:(tt + 1) * P], cw[:, 3, :])
                i.then_inc(c_wo.sem, 1)
                yield
                pe.wait_ge(b_xn.sem, b_xn.at(s, 2))
                turn_tiles(bb[2], lambda tt: bxn[:, tt, :]).then_inc(b_tp.sem, 1)
                yield
                pe.wait_ge(b_xt.sem, b_xt.at(s, 2))
                for tt in range(NT):
                    i = mm(bb[3][:, tt * EXPERTS:(tt + 1) * EXPERTS], bxt[:, tt * P:(tt + 1) * P], gw[:, :])
                i.then_inc(r_l.sem, 1)
                yield

                def down(e):
                    pe.wait_ge(m_hid.sem, m_hid.at(s, 2 * e + 2))
                    if e == 0:
                        pe.wait_ge(r_m.sem, r_m.at(s, 1))
                    else:
                        pe.wait_ge(m_sum.sem, m_sum.at(s, e))
                    for tt in range(NT):
                        for c in range(2):
                            i = mm(bb[3][:, tt * P:(tt + 1) * P], hid[e % 2][:, c, tt * P:(tt + 1) * P],
                                   mw[:, e % SLOTS, 2 * MH + c * P:2 * MH + (c + 1) * P], start=(c == 0), stop=(c == 1))
                    i.then_inc(m_d.sem, 1)

                for e in range(ALL):
                    pe.wait_ge(s_mw[e % SLOTS].sem, s_mw[e % SLOTS].at(s, e // SLOTS + 1))
                    for c in range(2):
                        for j, done in ((0, m_g), (1, m_u)):
                            n = 4 * e + 2 * c + j
                            if n >= 3:
                                q = n - 3
                                read = m_hid if q % 2 else m_silu
                                pe.wait_ge(read.sem, read.at(s, q // 2 + 1))
                            mm(bb[n % 3], mw[:, e % SLOTS, j * MH + c * P:j * MH + (c + 1) * P], bxt[:, :]).then_inc(done.sem, 1)
                    if e:
                        down(e - 1)
                    yield
                down(ALL - 1)
                yield

            run_halves(pe, front, back)

        @block.scalar
        def _(act):
            def norm_inverse(s, k, stats, rstd, mv, rs, order):
                act.wait_ge(stats.sem, stats.at(s, k))
                nc.scalar.activation(rs[:, 0, :], mv[:, :, 1], ACT.Ln, bias=consts[:, 0:1]).then_inc(order.sem, order.one())
                act.wait_ge(order.sem, order.now(s))
                nc.scalar.activation(rs[:, 1, :], rs[:, 0, :], ACT.Exp, scale=-0.5).then_inc(rstd.sem, 1)

            def front(s):
                fa.start()
                norm_inverse(s, 1, f_stats, f_rstd, fmv, frs, fa)
                yield
                act.wait_ge(f_tp.sem, f_tp.at(s, 1))
                nc.scalar.copy(axt, fb[0][:, :]).then_inc(f_xt.sem, 1)
                yield
                act.wait_ge(a_qkv.sem, a_qkv.at(s, 1))
                nc.scalar.activation(aqt, fb[1][:, :], ACT.Identity, bias=abq[:, 0:1], scale=float(T) ** -0.5).then_inc(a_qk.sem, 1)
                act.wait_ge(a_qkv.sem, a_qkv.at(s, 2))
                nc.scalar.activation(akt, fb[2][:, :], ACT.Identity, bias=ab[:, 1:2]).then_inc(a_qk.sem, 1)
                yield
                for b in range(NT):
                    act.wait_ge(a_max.sem, a_max.at(s, b + 1))
                    nc.scalar.activation(ae[:, b, :], fb[b][:, :], ACT.Exp, bias=am[:, b:b + 1],
                                                       accum_out=asum[:, b:b + 1]).then_inc(a_e.sem, 1)
                norm_inverse(s, 2, f_stats, f_rstd, fmv, frs, fa)
                yield
                act.wait_ge(f_tp.sem, f_tp.at(s, 2))
                nc.scalar.copy(h[0:64, 0:T], fb[0][0:64, :])
                nc.scalar.copy(h[64:128, 1:T + 1], fb[0][64:128, :]).then_inc(f_xt.sem, 1)
                yield
                for l in range(LAYERS):
                    for tt in range(NT):
                        for j in range(3):
                            n = 3 * tt + j
                            act.wait_ge(l_qkv.sem, l_qkv.at(s, 12 * l + n + 1))
                            if j < 2:
                                nc.scalar.copy(qk[:, tt, j * INNER:(j + 1) * INNER], fb[n % 4][:, :]).then_inc(l_ev.sem, 1)
                            else:
                                nc.scalar.copy(v[:, tt, :], fb[n % 4][:, :]).then_inc(l_ev.sem, 1)
                        act.wait_ge(l_ev.sem, l_ev.at(s, 12 * l + 3 * tt + 2))
                        if tt:
                            act.wait_ge(l_ss.sem, l_ss.at(s, 4 * l + tt))
                        nc.scalar.activation(sq, qk[:, tt, :], ACT.Square).then_inc(l_sq.sem, 1)
                        if tt == 1:
                            yield
                    act.wait_ge(l_ssc.sem, l_ssc.at(s, l + 1))
                    nc.scalar.activation(rn[:, :, :], ss[:, :, :], ACT.Ln).then_inc(fa.sem, fa.one())
                    act.wait_ge(fa.sem, fa.now(s))
                    nc.scalar.activation(rn[:, :, :], rn[:, :, :], ACT.Exp, scale=-0.5, bias=consts[:, 1:2]).then_inc(l_rn.sem, 1)
                    yield
                    for tt in range(NT):
                        act.wait_ge(l_tq.sem, l_tq.at(s, 4 * l + tt + 1))
                        nc.scalar.copy(qt[:, :, tt * P:(tt + 1) * P],
                                                      fb[2 * tt % 4][:, :].rearrange("p (a b) -> p a b", b=P)).then_inc(l_qt.sem, 1)
                        if tt == 1:
                            yield
                    yield
                    for f in range(2 * NP):
                        act.wait_ge(l_max.sem, l_max.at(s, 8 * l + f + 1))
                        for j in range(4):
                            k = 4 * f + j
                            i = nc.scalar.activation(pr[:, f, j, :], fb[f % 4][:, j * P:(j + 1) * P], ACT.Exp,
                                                     bias=pmax[:, k:k + 1], accum_out=psum_[:, k:k + 1])
                        i.then_inc(l_exp.sem, 1)
                        if f == 3:
                            yield
                    yield
                    for f in (1, 3, 5, 7):
                        act.wait_ge(l_pt.sem, l_pt.at(s, 8 * l + f + 1))
                        nc.scalar.copy(pt[:, f, :, :].rearrange("p a b -> p (a b)"), fb[f % 4][:, :]).then_inc(l_pta.sem, 1)
                        if f == 3:
                            yield
                    for p in (0, 1):
                        act.wait_ge(l_pv.sem, l_pv.at(s, 4 * l + p + 1))
                        nc.scalar.copy(qt[:, p, :], fb[p][:, :]).then_inc(l_ot.sem, 1)
                    yield
                    for p in (2, 3):
                        act.wait_ge(l_pv.sem, l_pv.at(s, 4 * l + p + 1))
                        nc.scalar.copy(qt[:, p, :], fb[p][:, :]).then_inc(l_ot.sem, 1)
                    yield
                    yield
                    act.wait_ge(l_dc.sem, l_dc.at(s, l + 1))
                    nc.scalar.activation(dsq, dc, ACT.Square).then_inc(l_dsq.sem, 1)
                    yield
                    act.wait_ge(l_var.sem, l_var.at(s, l + 1))
                    nc.scalar.activation(drs, fb[2][:, :], ACT.Ln, bias=consts[:, 0:1]).then_inc(fa.sem, fa.one())
                    act.wait_ge(fa.sem, fa.now(s))
                    nc.scalar.activation(drs, drs, ACT.Exp, scale=-0.5).then_inc(l_drs.sem, 1)
                    act.wait_ge(l_dn.sem, l_dn.at(s, l + 1))
                    nc.scalar.activation(hn, dc, ACT.Identity, bias=lnb[:, l:l + 1], scale=lng[:, l:l + 1]).then_inc(l_hn.sem, 1)
                    yield
                    for c in range(HC):
                        act.wait_ge(l_g.sem, l_g.at(s, 3 * l + c + 1))
                        if c == 2:
                            act.wait_ge(l_hg.sem, l_hg.at(s, 3 * l + 1))
                        nc.scalar.activation(gel[c % 2], fb[2 * c % 4][0:HT, :], ACT.Gelu,
                                                              bias=b1[:, l, 1, c:c + 1]).then_inc(l_gelu.sem, 1)
                    yield
                    yield
                yield
                finish(fa)

            def back(s, last=False):
                ba.start()
                norm_inverse(s, 1, b_stats, b_rstd, bmv, brs, ba)
                yield
                act.wait_ge(b_tp.sem, b_tp.at(s, 1))
                nc.scalar.copy(bxt[:, :], bb[0][:, :]).then_inc(b_xt.sem, 1)
                yield
                act.wait_ge(c_qkv.sem, c_qkv.at(s, 1))
                nc.scalar.activation(qkf[:, 0, :], bb[1][:, :], ACT.Copy, scale=float(CD) ** -0.5).then_inc(c_qkf.sem, 1)
                act.wait_ge(c_qkv.sem, c_qkv.at(s, 2))
                nc.scalar.copy(qkf[:, 1, :], bb[2][:, :]).then_inc(c_qkf.sem, 1)
                yield
                for r in range(2):
                    yield
                    yield
                    yield
                    yield

                    def exps(g):
                        gg = 2 * r + g
                        if gg:
                            act.wait_ge(c_pv.sem, c_pv.at(s, gg))
                        for n in range(len(EXP_FILLS)):
                            k = 10 * gg + n
                            act.wait_ge(c_s2.sem, c_s2.at(s, k + 1))
                            nc.scalar.activation(big[:, n, :], bb[k % 20 % 3][:, :], ACT.Exp).then_inc(c_e.sem, 1)

                    exps(0)
                    yield
                    act.wait_ge(c_pv.sem, c_pv.at(s, 2 * r + 1))
                    nc.scalar.copy(oc[:, 2 * r, :], bb[3][:, :]).then_inc(c_oc.sem, 1)
                    exps(1)
                    yield
                    act.wait_ge(c_pv.sem, c_pv.at(s, 2 * r + 2))
                    nc.scalar.copy(oc[:, 2 * r + 1, :], bb[3][:, :]).then_inc(c_oc.sem, 1)
                    yield
                yield
                act.wait_ge(c_ont.sem, c_ont.at(s, 1))
                nc.scalar.copy(ont[:, :], bb[0][:, :]).then_inc(c_onx.sem, 1)
                yield
                norm_inverse(s, 2, b_stats, b_rstd, bmv, brs, ba)
                yield
                act.wait_ge(b_tp.sem, b_tp.at(s, 2))
                nc.scalar.copy(bxt[:, :], bb[2][:, :]).then_inc(b_xt.sem, 1)
                yield
                act.wait_ge(r_m.sem, r_m.at(s, 1))
                nc.scalar.activation(rt[:, 1, :, :], rt[:, 0, :, :], ACT.Exp).then_inc(r_e.sem, 1)
                yield
                for e in range(ALL):
                    for c in range(2):
                        n = 4 * e + 2 * c
                        act.wait_ge(m_g.sem, m_g.at(s, 2 * e + c + 1))
                        if e >= 2:
                            act.wait_ge(m_hid.sem, m_hid.at(s, 2 * e - 3 + c))
                        elif e == 0 and c == 0:
                            act.wait_ge(c_pv.sem, c_pv.at(s, 4))
                        nc.scalar.activation(silu[e % 2][:, c, :], bb[n % 3][:, :], ACT.Silu).then_inc(m_silu.sem, 1)
                    yield
                yield
                finish(ba)

            run_halves(act, front, back)

        @block.vector
        def _(dve):
            tt_, ts, stt, cp = nc.vector.tensor_tensor, nc.vector.tensor_scalar, nc.vector.scalar_tensor_tensor, nc.vector.tensor_copy
            dve.wait_ge(loaded, 16 * n_loads)
            dve.wait_ge(x3_free, 16)
            for l in range(LAYERS):
                for j in range(2):
                    tt_(cosT[:, l, :, j, :], cs_in[:, 0, :, j, :],
                        qks[:, l, j, :].unsqueeze(1).broadcast_to([P, NT, DH]), ALU.mult)
                    for z in range(2):
                        tt_(sinT[:, l, :, j, 32 * z:32 * z + 32], cs_in[:, 1, :, j, 32 * z:32 * z + 32],
                            qks[:, l, j, 32 - 32 * z:64 - 32 * z].unsqueeze(1).broadcast_to([P, NT, 32]), ALU.mult)
            ts(abq[:, :], ab[:, 0:1], float(T) ** -0.5, None, ALU.mult)
            cp(maskb[:, :], maskf)
            cp(identb[:, :], ident[:, :])
            nc.vector.memset(consts[:, 0:1], EPS)
            nc.vector.memset(consts[:, 1:2], 8.0 * float(np.log(2.0))).then_inc(ready_v, 1)
            dve.wait_ge(ready_v, 1)
            dve.wait_ge(ready_p, 2)

            def moments(s, k, src, st, mv, stats, order):
                for tt in range(NT):
                    i = nc.vector.bn_stats(st[:, tt, :], src[:, tt, :])
                i.then_inc(order.sem, order.one())
                dve.wait_ge(order.sem, order.now(s))
                nc.vector.memset(pause[:, :], 0.0)
                for tt in range(NT):
                    i = nc.vector.bn_aggr(mv[:, tt, :], st[:, tt, :])
                i.then_inc(stats.sem, 1)
                dve.wait_ge(stats.sem, stats.at(s, k))

            def normalise(s, k, src, xn, mv, rs, rstd, out_sig):
                dve.wait_ge(rstd.sem, rstd.at(s, k))
                for tt in range(NT):
                    i = ts(xn[:, tt, :], src[:, tt, :], mv[:, tt, 0:1], rs[:, 1, tt:tt + 1], ALU.subtract, ALU.mult)
                i.then_inc(out_sig.sem, 1)

            def front(s):
                fv.start()
                dve.wait_ge(s_x.sem, s_x.at(s, 1))
                moments(s, 1, xin, fst, fmv, f_stats, fv)
                normalise(s, 1, xin, fxn, fmv, frs, f_rstd, f_xn)
                yield
                yield
                dve.wait_ge(a_qkv.sem, a_qkv.at(s, 3))
                tt_(av, fb[3][:, :].rearrange("p (a b) -> p a b", a=NT),
                                  abv[:, :].unsqueeze(1).broadcast_to([P, NT, P]), ALU.add).then_inc(a_v.sem, 1)
                yield
                for b in range(NT):
                    dve.wait_ge(a_s.sem, a_s.at(s, b + 1))
                    nc.vector.tensor_reduce(am[:, b:b + 1], fb[b][:, :], AX.X, ALU.max, negate=True).then_inc(a_max.sem, 1)
                dve.wait_ge(a_e.sem, a_e.at(s, 4))
                tt_(adj, aed, ident[:, :].unsqueeze(1).broadcast_to([P, NT, P]), ALU.mult).then_inc(fv.sem, fv.one())
                dve.wait_ge(fv.sem, fv.now(s))
                nc.vector.tensor_reduce(adiag, adj, AX.X, ALU.add).then_inc(fv.sem, fv.one())
                nc.vector.reciprocal(arec, asum).then_inc(fv.sem, fv.one())
                dve.wait_ge(fv.sem, fv.now(s))
                tt_(adiag, adiag, arec, ALU.mult).then_inc(fv.sem, fv.one())
                dve.wait_ge(fv.sem, fv.now(s))
                for tt in range(NT):
                    i = stt(out=x1[:, tt, :], in0=av[:, tt, :], scalar=adiag[:, tt:tt + 1], in1=xin[:, tt, :],
                            op0=ALU.mult, op1=ALU.add)
                i.then_inc(a_x1.sem, 1)
                dve.wait_ge(a_x1.sem, a_x1.at(s, 1))
                moments(s, 2, x1, fst, fmv, f_stats, fv)
                normalise(s, 2, x1, fxn, fmv, frs, f_rstd, f_xn)
                yield
                yield
                for l in range(LAYERS):
                    for tt in range(NT):
                        dve.wait_ge(l_ev.sem, l_ev.at(s, 12 * l + 3 * tt + 2))
                        if tt >= 2:
                            dve.wait_ge(l_add.sem, l_add.at(s, 4 * l + tt - 1))
                        for j in range(2):
                            q4 = qk[:, tt, j * INNER:(j + 1) * INNER].rearrange("p (a z c) -> p a z c", z=2, c=32)
                            p4 = part[tt % 2][:, j * INNER:(j + 1) * INNER].rearrange("p (a z c) -> p a z c", z=2, c=32)
                            t4 = sinT[:, l, tt, j, :].rearrange("p (z c) -> p z c", z=2)
                            i = tt_(p4, q4[:, :, ::-1, :], t4.unsqueeze(1).broadcast_to([P, HEADS, 2, 32]), ALU.mult)
                        i.then_inc(fv.sem, fv.one())
                        dve.wait_ge(l_sq.sem, l_sq.at(s, 4 * l + tt + 1))
                        nc.vector.tensor_reduce(ss[:, tt, :], sq.rearrange("p (a b) -> p a b", b=DH), AX.X, ALU.add).then_inc(l_ss.sem, 1)
                        q4 = qk[:, tt, :].rearrange("p (j a c) -> p j a c", j=2, c=DH)
                        dve.wait_ge(fv.sem, fv.now(s))
                        tt_(q4, q4, cosT[:, l, tt, :, :].unsqueeze(2).broadcast_to([P, 2, HEADS, DH]), ALU.mult).then_inc(l_rot.sem, 1)
                        if tt == 1:
                            yield
                    dve.wait_ge(l_ss.sem, l_ss.at(s, 4 * l + 4))
                    ts(ss[:, :, :], ss[:, :, :], 1e-24, 65536.0, ALU.max, ALU.mult).then_inc(l_ssc.sem, 1)
                    yield
                    for tt in range(NT):
                        dve.wait_ge(l_tk.sem, l_tk.at(s, 4 * l + tt + 1))
                        src = fb[(2 * tt + 1) % 4][:, :].rearrange("p (a b) -> p a b", b=P)
                        lo = WINDOW + tt * P
                        cp(kt[0:64, :, 0, lo:lo + P], src[0:64])
                        cp(kt[64:128, :, 1, lo:lo + P], src[64:128]).then_inc(l_kt.sem, 1)
                        if tt == 1:
                            yield
                    yield
                    def reciprocals(f):
                        dve.wait_ge(l_exp.sem, l_exp.at(s, 8 * l + f + 1))
                        nc.vector.reciprocal(prec[:, 4 * f:4 * f + 4], psum_[:, 4 * f:4 * f + 4]).then_inc(l_rec.sem, 1)
                    for f in range(2 * NP):
                        dve.wait_ge(l_sim.sem, l_sim.at(s, 8 * l + f + 1))
                        nc.vector.tensor_reduce(pmax[:, 4 * f:4 * f + 4],
                                                                fb[f % 4][:, :].rearrange("p (a b) -> p a b", b=P),
                                                                AX.X, ALU.max, negate=True).then_inc(l_max.sem, 1)
                        if f >= 1:
                            reciprocals(f - 1)
                        if f == 3:
                            yield
                    reciprocals(7)
                    yield
                    for f in (0, 2, 4, 6):
                        dve.wait_ge(l_pt.sem, l_pt.at(s, 8 * l + f + 1))
                        cp(pt[:, f, :, :].rearrange("p a b -> p (a b)"), fb[f % 4][:, :]).then_inc(l_ptv.sem, 1)
                        if f == 2:
                            yield
                    yield
                    yield
                    dve.wait_ge(l_wo.sem, l_wo.at(s, l + 1))
                    tt_(h[0:64, 0:T], fb[0][0:64, :], h[0:64, 0:T], ALU.add)
                    tt_(h[64:128, 1:T + 1], fb[0][64:128, :], h[64:128, 1:T + 1], ALU.add).then_inc(l_h1.sem, 1)
                    yield
                    dve.wait_ge(l_mean.sem, l_mean.at(s, l + 1))
                    dve.wait_ge(l_h1.sem, l_h1.at(s, l + 1))
                    tt_(dc, hs, fb[1][:, :], ALU.subtract).then_inc(l_dc.sem, 1)
                    yield
                    dve.wait_ge(l_drs.sem, l_drs.at(s, l + 1))
                    tt_(dc, dc, drs, ALU.mult).then_inc(l_dn.sem, 1)
                    yield
                    for c in range(HC):
                        dve.wait_ge(l_a.sem, l_a.at(s, 3 * l + c + 1))
                        dve.wait_ge(l_gelu.sem, l_gelu.at(s, 3 * l + c + 1))
                        stt(out=hg[:, c, :], in0=fb[(2 * c + 1) % 4][0:HT, :], scalar=b1[:, l, 0, c:c + 1],
                                           in1=gel[c % 2], op0=ALU.add, op1=ALU.mult).then_inc(l_hg.sem, 1)
                    yield
                    dve.wait_ge(l_w2.sem, l_w2.at(s, l + 1))
                    lo_out, hi_out = (h[0:64, 0:T], h[64:128, 1:T + 1]) if l < LAYERS - 1 else (fin[0:64, :], fin[64:128, :])
                    stt(out=lo_out, in0=fb[2][0:64, :], scalar=b2[0:64, l:l + 1], in1=h[0:64, 0:T], op0=ALU.add, op1=ALU.add)
                    stt(out=hi_out, in0=fb[2][64:128, :], scalar=b2[64:128, l:l + 1], in1=h[64:128, 1:T + 1],
                                       op0=ALU.add, op1=ALU.add).then_inc(l_h2.sem, 1)
                    yield
                dve.wait_ge(f_ft.sem, f_ft.at(s, 1))
                tt_(x2[:, :, :], fb[3][:, :].rearrange("p (a b) -> p a b", a=NT), x1[:, :, :], ALU.add).then_inc(f_x2.sem, 1)
                yield
                finish(fv)

            def back(s, last=False):
                bv.start()
                dve.wait_ge(f_x2.sem, f_x2.at(s, 1))
                moments(s, 1, x2, bst, bmv, b_stats, bv)
                normalise(s, 1, x2, bxn, bmv, brs, b_rstd, b_xn)
                yield
                yield
                dve.wait_ge(c_qkf.sem, c_qkf.at(s, 2))
                cp(parts[:, 0, :, :], qkf).then_inc(bv.sem, bv.one())
                dve.wait_ge(bv.sem, bv.now(s))
                tt_(qkr, qkf, parts[:, 0, :, :], ALU.subtract).then_inc(bv.sem, bv.one())
                dve.wait_ge(bv.sem, bv.now(s))
                cp(parts[:, 1, :, :], qkr).then_inc(bv.sem, bv.one())
                dve.wait_ge(bv.sem, bv.now(s))
                tt_(parts[:, 2, :, :], qkr, parts[:, 1, :, :], ALU.subtract).then_inc(c_parts.sem, 1)
                dve.wait_ge(c_qkv.sem, c_qkv.at(s, 3))
                cp(va[:, :, :, 0:CD], bb[3][:, :].rearrange("p (a b c) -> p a b c", a=NT, c=CD)).then_inc(c_v.sem, 1)
                yield
                for r in range(2):
                    yield
                    for n, (t, heads) in enumerate(MAX_FILLS):
                        cols = (t + 1) * P
                        dve.wait_ge(c_s1.sem, c_s1.at(s, 22 * r + n + 1))
                        nc.vector.tensor_reduce(
                            cmax[:, r, heads[0]:heads[-1] + 1, t],
                            bb[n % 4][:, 0:cols * len(heads)].rearrange("p (a b) -> p a b", b=cols), AX.X, ALU.max, negate=True).then_inc(c_m.sem, 1)
                        if n == 10:
                            yield
                    yield
                    dve.wait_ge(c_mt.sem, c_mt.at(s, r + 1))
                    m = bb[0][0:RH * NT, 0:P]
                    cp(mrow[:, 0, :], m).then_inc(bv.sem, bv.one())
                    dve.wait_ge(bv.sem, bv.now(s))
                    tt_(mrem[:, 0, :], m, mrow[:, 0, :], ALU.subtract).then_inc(bv.sem, bv.one())
                    dve.wait_ge(bv.sem, bv.now(s))
                    cp(mrow[:, 1, :], mrem[:, 0, :]).then_inc(bv.sem, bv.one())
                    dve.wait_ge(bv.sem, bv.now(s))
                    tt_(mrow[:, 2, :], mrem[:, 0, :], mrow[:, 1, :], ALU.subtract).then_inc(c_mr.sem, 1)
                    yield
                    yield
                    yield
                    yield
                for tt in range(NT):
                    dve.wait_ge(c_ot.sem, c_ot.at(s, tt + 1))
                    o4 = bb[tt][:, :].rearrange("p (a b) -> p a b", b=32)
                    nc.vector.reciprocal(crec[:, :], o4[:, :, CD]).then_inc(bv.sem, bv.one())
                    dve.wait_ge(bv.sem, bv.now(s))
                    tt_(on[:, tt, :].rearrange("p (a b) -> p a b", b=CD), o4[:, :, 0:CD],
                                       crec[:, :].unsqueeze(2).broadcast_to([P, CH, CD]), ALU.mult).then_inc(c_on.sem, 1)
                    dve.wait_ge(c_on.sem, c_on.at(s, tt + 1))
                yield
                yield
                dve.wait_ge(c_wo.sem, c_wo.at(s, 1))
                dve.wait_ge(x3_free, 16 * (s + 1))
                tt_(x3[:, :, :], bb[1][:, :].rearrange("p (a b) -> p a b", a=NT), x2[:, :, :], ALU.add).then_inc(c_x3.sem, 1)
                dve.wait_ge(c_x3.sem, c_x3.at(s, 1))
                moments(s, 2, x3, bst, bmv, b_stats, bv)
                normalise(s, 2, x3, bxn, bmv, brs, b_rstd, b_xn)
                yield
                yield
                lg = bb[3][:, 0:NT * EXPERTS].rearrange("p (a b) -> p a b", a=NT)
                wide = lambda x: x.unsqueeze(2).broadcast_to([P, NT, EXPERTS])
                dve.wait_ge(r_l.sem, r_l.at(s, 1))
                nc.vector.tensor_reduce(rs1[:, 0, :], lg, AX.X, ALU.max).then_inc(bv.sem, bv.one())
                dve.wait_ge(bv.sem, bv.now(s))
                tt_(rt[:, 0, :, :], lg, wide(rs1[:, 0, :]), ALU.subtract).then_inc(r_m.sem, 1)
                dve.wait_ge(r_e.sem, r_e.at(s, 1))
                nc.vector.tensor_reduce(rs1[:, 1, :], rt[:, 1, :, :], AX.X, ALU.add).then_inc(bv.sem, bv.one())
                dve.wait_ge(bv.sem, bv.now(s))
                nc.vector.reciprocal(rs1[:, 2, :], rs1[:, 1, :]).then_inc(bv.sem, bv.one())
                dve.wait_ge(bv.sem, bv.now(s))
                tt_(rt[:, 2, :, :], rt[:, 1, :, :], wide(rs1[:, 2, :]), ALU.mult).then_inc(bv.sem, bv.one())
                dve.wait_ge(bv.sem, bv.now(s))
                nc.vector.memset(pause[:, :], 0.0)
                for tt in range(NT):
                    i = nc.vector.max(rt[:, 3, tt, :], rt[:, 2, tt, :])
                i.then_inc(bv.sem, bv.one())
                dve.wait_ge(bv.sem, bv.now(s))
                nc.vector.memset(pause[:, :], 0.0)
                for tt in range(NT):
                    i = nc.vector.max_index(rti[:, tt, :], rt[:, 3, tt, :], rt[:, 2, tt, :])
                i.then_inc(bv.sem, bv.one())
                dve.wait_ge(bv.sem, bv.now(s))
                cp(rt[:, 4, :, :], rti[:, :, :]).then_inc(bv.sem, bv.one())
                tt_(rs1[:, 3, :], rt[:, 3, :, 0], rt[:, 3, :, 1], ALU.add).then_inc(bv.sem, bv.one())
                dve.wait_ge(bv.sem, bv.now(s))
                ts(rs1[:, 3, :], rs1[:, 3, :], 1e-20, None, ALU.add).then_inc(bv.sem, bv.one())
                dve.wait_ge(bv.sem, bv.now(s))
                nc.vector.reciprocal(rs1[:, 2, :], rs1[:, 3, :]).then_inc(bv.sem, bv.one())
                dve.wait_ge(bv.sem, bv.now(s))
                ids = iota[:, :].unsqueeze(1).broadcast_to([P, NT, EXPERTS])
                for k in range(2):
                    tt_(rt[:, 5 + k, :, :], ids, wide(rt[:, 4, :, k]), ALU.is_equal).then_inc(bv.sem, bv.one())
                dve.wait_ge(bv.sem, bv.now(s))
                for k in range(2):
                    tt_(rt[:, 5 + k, :, :], rt[:, 5 + k, :, :], wide(rt[:, 3, :, k]), ALU.mult).then_inc(bv.sem, bv.one())
                dve.wait_ge(bv.sem, bv.now(s))
                tt_(rt[:, 7, :, :], rt[:, 5, :, :], rt[:, 6, :, :], ALU.add).then_inc(bv.sem, bv.one())
                dve.wait_ge(bv.sem, bv.now(s))
                tt_(gate[:, :, :], rt[:, 7, :, :], wide(rs1[:, 2, :]), ALU.mult).then_inc(r_w.sem, 1)
                dve.wait_ge(r_w.sem, r_w.at(s, 1))
                yield

                def add_expert(e):
                    dve.wait_ge(m_d.sem, m_d.at(s, e + 1))
                    if e:
                        dve.wait_ge(m_sum.sem, m_sum.at(s, e))
                    if e == EXPERTS:
                        tt_(outb[:, :, :], bb[3][:, :].rearrange("p (a b) -> p a b", a=NT), outb[:, :, :], ALU.add).then_inc(m_sum.sem, 1)
                        return
                    for tt in range(NT):
                        i = stt(out=outb[:, tt, :], in0=bb[3][:, tt * P:(tt + 1) * P], scalar=gate[:, tt, e:e + 1],
                                in1=outb[:, tt, :], op0=ALU.mult, op1=ALU.add)
                    i.then_inc(m_sum.sem, 1)

                for e in range(ALL):
                    for c in range(2):
                        n = 4 * e + 2 * c + 1
                        dve.wait_ge(m_u.sem, m_u.at(s, 2 * e + c + 1))
                        dve.wait_ge(m_silu.sem, m_silu.at(s, 2 * e + c + 1))
                        if e >= 2 and c == 0:
                            dve.wait_ge(m_d.sem, m_d.at(s, e - 1))
                        tt_(hid[e % 2][:, c, :], bb[n % 3][:, :], silu[e % 2][:, c, :], ALU.mult).then_inc(m_hid.sem, 1)
                    if e:
                        add_expert(e - 1)
                    yield
                add_expert(ALL - 1)
                yield
                finish(bv)

            run_halves(dve, front, back)

        @block.gpsimd
        def _(pool):
            nc.gpsimd.memset(h[:, :], 0.0)
            nc.gpsimd.memset(kt[:, :, :, :], 0.0)
            nc.gpsimd.memset(v2[:, 0, :], 0.0)
            nc.gpsimd.memset(va[:, :, :, CD + 1:32], 0.0)
            nc.gpsimd.memset(va[:, :, :, CD:CD + 1], 1.0)
            nc.gpsimd.memset(mean_w[:, :], 1.0 / P)
            nc.gpsimd.memset(pq[:, :, :], 0.0)
            nc.gpsimd.memset(pk[:, :, :], 0.0).then_inc(ready_p, 1)
            pool.wait_ge(ready_p, 1)
            nc.gpsimd.memset(pk[96:99, :, :], 1.0).then_inc(ready_p, 1)

            def front(s):
                for _ in range(5):
                    yield
                for l in range(LAYERS):
                    for tt in range(NT):
                        pool.wait_ge(l_rot.sem, l_rot.at(s, 4 * l + tt + 1))
                        nc.gpsimd.tensor_tensor(qk[:, tt, :], qk[:, tt, :], part[tt % 2], ALU.add).then_inc(l_add.sem, 1)
                        if tt == 1:
                            yield
                    yield
                    pool.wait_ge(l_rn.sem, l_rn.at(s, l + 1))
                    pool.wait_ge(l_add.sem, l_add.at(s, 4 * l + 4))
                    for tt in range(NT):
                        q3 = qk[:, tt, :].rearrange("p (a b) -> p a b", b=DH)
                        nc.gpsimd.tensor_tensor(q3, q3, rn[:, tt, :].unsqueeze(2).broadcast_to([P, 2 * HEADS, DH]), ALU.mult).then_inc(l_qkn.sem, 1)
                        if tt == 1:
                            yield
                    yield
                    for f in range(2 * NP):
                        pool.wait_ge(l_rec.sem, l_rec.at(s, 8 * l + f + 1))
                        nc.gpsimd.tensor_tensor(pr[:, f, :, :], pr[:, f, :, :],
                                                               prec[:, 4 * f:4 * f + 4].unsqueeze(2).broadcast_to([P, 4, P]), ALU.mult).then_inc(l_pn.sem, 1)
                        if f == 3:
                            yield
                    yield
                    for _ in range(8):
                        yield
                yield

            def back(s, last=False):
                for _ in BACK:
                    yield

            run_halves(pool, front, back)

        @block.sync
        def _(sp):
            for dst, src in loads:
                sp.dma_start(dst, src).then_inc(loaded, 16)
            sp.dma_start(qks[:, :, :, :], io["qk_scale"].unsqueeze(0).broadcast_to([P, LAYERS, 2, DH])).then_inc(x3_free, 16)

            def front(s):
                if not isinstance(s, int) or s:
                    sp.wait_ge(a_x1.sem, a_x1.at(s - 1, 1))
                sp.dma_start(xin[:, :, :], io["x"][bass.ds(s, 1), :, :].rearrange("o (a p) e -> p (o a) e", p=P)).then_inc(s_x.sem, 16)
                for _ in range(5):
                    yield
                for l in range(LAYERS):
                    yield
                    sp.wait_ge(l_ev.sem, l_ev.at(s, 12 * l + 12))
                    sp.dma_start(v2[64:128, :, :], v[0:64, :, :]).then_inc(l_v2.sem, 16)
                    sp.dma_start(v2[0:64, 1:NT, :], v[64:128, 0:NT - 1, :]).then_inc(l_v2.sem, 16)
                    for _ in range(13):
                        yield
                yield

            def load_expert(e):
                sp.dma_start(mw[:, e % SLOTS, :], io["experts"][e, :, :]).then_inc(s_mw[e % SLOTS].sem, 16)

            for e in range(SLOTS):
                load_expert(e)

            def back(s, last=False):
                yield
                yield
                sp.wait_ge(c_parts.sem, c_parts.at(s, 1))
                sp.dma_start(scr.rearrange("k j h d t -> (h d) k j t"), parts).then_inc(c_saved.sem, 16)
                yield
                for r in range(2):
                    sp.wait_ge(c_saved.sem, c_saved.at(s, 1))
                    if r:
                        sp.wait_ge(c_s2.sem, c_s2.at(s, 20))
                    hs_ = slice(r * RH, (r + 1) * RH)
                    for b in range(9):
                        for j, dst, k in ((0, pq, b // 3), (1, pk, b % 3)):
                            sp.dma_start(dst[CD * b:CD * (b + 1), :, :],
                                                            scr[k, j, hs_, :, :].rearrange("h d t -> d h t")).then_inc(c_packed.sem, 16)
                    yield
                    yield
                    yield
                    sp.wait_ge(c_mr.sem, c_mr.at(s, r + 1))
                    sp.dma_start(scrm.rearrange("k a b -> a k b"), mrow[:, :, :]).then_inc(c_msaved.sem, 16)
                    sp.wait_ge(c_msaved.sem, c_msaved.at(s, r + 1))
                    sp.dma_start(pq[96:99, :, :], scrm.rearrange("k (a c) b -> k a (c b)", a=RH)).then_inc(c_mpacked.sem, 16)
                    yield
                    yield
                    yield
                    yield
                for _ in range(5):
                    yield
                for e in range(ALL):
                    if e:
                        if e + SLOTS - 1 < ALL:
                            sp.wait_ge(m_d.sem, m_d.at(s, e))
                            load_expert(e - 1 + SLOTS)
                        elif not last:
                            sp.wait_ge(m_d.sem, m_d.at(s, e))
                            load_expert((e - 1 + SLOTS) % ALL)
                    yield
                if not last:
                    sp.wait_ge(m_d.sem, m_d.at(s, ALL))
                    load_expert(SLOTS - 1)
                sp.wait_ge(m_sum.sem, m_sum.at(s, ALL))
                sp.dma_start(out[bass.ds(s, 1), :, :].rearrange("o (a p) e -> p (o a) e", p=P), outb[:, :, :]).then_inc(x3_free, 16)
                yield

            run_halves(sp, front, back)
            sp.wait_ge(x3_free, 16 * (SEQS + 1))


def rotary_factors():
    half = np.arange(0, DH, 2, dtype=np.float32)
    inv = (1.0 / 10000.0 ** (half / DH)).astype(np.float32)
    t = np.arange(T, dtype=np.float32)
    freqs = np.concatenate([t[:, None] * inv[None, :]] * 2, -1).astype(np.float64)
    base = (half + 0.4 * DH) / (1.4 * DH)
    power = (t - T // 2) / float(WINDOW // 2)
    scale = np.concatenate([base.astype(np.float64)[None, :] ** power[:, None]] * 2, -1)
    sign = np.where(np.arange(DH) < DH // 2, -1.0, 1.0)
    out = np.empty((2, T, 2, DH))
    for j, factor in ((0, 8.0 * scale), (1, 1.0 / scale)):
        out[0, :, j, :] = np.cos(freqs) * factor
        out[1, :, j, :] = np.sin(freqs) * factor * sign
    return np.ascontiguousarray(out.reshape(2, NT, P, 2, DH).transpose(2, 0, 1, 3, 4).astype(np.float32))


def masks():
    i, j = np.arange(P)[:, None] % WINDOW, np.arange(P)[None, :]
    keep = np.where(j < WINDOW, i <= j, j - WINDOW <= i)
    first = keep & ((np.arange(P)[:, None] >= WINDOW) | (j >= WINDOW))
    q, k = np.arange(P)[:, None], np.arange(P)[None, :]
    kept = np.concatenate([first, first, keep, keep] + [keep] * 4 + [k <= q, q <= k], 1)
    return np.where(kept, 0.0, NEG).astype(np.float32)


def kernel(**inputs):
    from concourse import bacc
    from concourse.bass_utils import run_bass_kernel_spmd

    a = {k: np.asarray(x) for k, x in inputs.items()}
    pad = lambda x, axis: np.concatenate([x, np.zeros_like(np.take(x, [0], axis))], axis)
    w1 = a["L0_ffn_w1"].reshape(LAYERS, P, 2, HID)
    b1 = a["L0_ffn_b1"].reshape(LAYERS, 2, HID)
    gate = np.concatenate([a["L1_ffn_w_gate"], a["L1_ffn_ws_gate"][None]])
    up = np.concatenate([a["L1_ffn_w_up"], a["L1_ffn_ws_up"][None]])
    down = np.concatenate([a["L1_ffn_w_down"], a["L1_ffn_ws_down"][None]])
    arrays = {
        "x": a["L0_attn_X_embed"],
        "aw": np.stack([a["L0_attn_W" + n].T for n in "qkv"], 1),
        "ab": np.stack([a["L0_attn_b" + n] for n in "qkv"], 1),
        "abv": a["L0_attn_bv"],
        "wqkv": a["L0_ffn_wqkv"],
        "wo": a["L0_ffn_wo"],
        "w1": pad(w1, 3).reshape(LAYERS, P, 2, HC, HT).transpose(1, 0, 2, 3, 4),
        "w2": pad(a["L0_ffn_w2"], 1).reshape(LAYERS, HC, HT, P).transpose(2, 0, 1, 3),
        "b1": pad(b1, 2).reshape(LAYERS, 2, HC, HT).transpose(3, 0, 1, 2),
        "b2": a["L0_ffn_b2"].T,
        "ln_g": a["L0_ffn_ln_g"].T,
        "ln_b": a["L0_ffn_ln_b"].T,
        "qk_scale": np.stack([a["L0_ffn_q_scale"], a["L0_ffn_k_scale"]], 1),
        "cw": np.stack([a["L1_attn_W" + n].T for n in "qkvo"], 1),
        "gate_w": a["L1_ffn_gate_w"],
        "experts": np.concatenate([gate, up, down.reshape(ALL, 2, P, P).transpose(0, 2, 1, 3).reshape(ALL, P, MH)], 2),
        "ident": np.eye(P, dtype=np.float32),
        "masks": masks(),
        "rotary": rotary_factors(),
        "iota": np.broadcast_to(np.arange(EXPERTS, dtype=np.float32), (P, EXPERTS)),
    }
    arrays = {k: np.ascontiguousarray(x) for k, x in arrays.items()}
    nc = bacc.Bacc("TRN2", target_bir_lowering=False, num_devices=1)
    io = {k: nc.dram_tensor(f"in_{k}", x.shape, mybir.dt.from_np(x.dtype), kind="ExternalInput").ap() for k, x in arrays.items()}
    out = nc.dram_tensor("out", (SEQS, T, P), F32, kind="ExternalOutput").ap()
    program(nc, io, out)
    result = run_bass_kernel_spmd(nc, [{f"in_{k}": x for k, x in arrays.items()}], core_ids=[0])
    return result.results[0]["out"]
```
